# Optimizing a Trainium2 kernel written in Bass

```python
import numpy as np
import jax
import jax.numpy as jnp

def _softmax(x, axis=-1):
    return jax.nn.softmax(x, axis=axis)

def _gelu(x):
    return jax.nn.gelu(x, approximate=True)

def _silu(x):
    return jax.nn.silu(x)

def _sigmoid(x):
    return jax.nn.sigmoid(x)

def _layernorm(x, axis=-1, eps=1e-05):
    m = jnp.mean(x, axis=axis, keepdims=True)
    v = jnp.var(x, axis=axis, keepdims=True)
    return (x - m) / jnp.sqrt(v + eps)

def _scatter_add(tgt, idx, src, axis=0):
    return tgt.at[idx].add(src)

def _segment_sum(src, seg, n):
    return jax.ops.segment_sum(src, seg, n)
kernel_name = 'mk_gnn_resnorm_d2_gnn_r32_876ff3'

def setup_inputs(seed: int=0):
    np.random.seed(seed)
    _w = jnp.asarray

    def _rec_inputs():
        import jax
        import jax.numpy as jnp
        _gk = jax.random.key(seed)
        x = -0.000202 + 1 * jax.random.normal(jax.random.fold_in(_gk, 1), (3125, 64), jnp.float32)
        _s = jax.random.randint(jax.random.fold_in(_gk, 2), (25000,), 0, 3125, jnp.int32)
        _d = jax.random.randint(jax.random.fold_in(_gk, 3), (25000,), 0, 3125, jnp.int32)
        _loop = jnp.arange(3125, dtype=jnp.int32)
        src = jnp.concatenate([_s, _d, _loop])
        dst = jnp.concatenate([_d, _s, _loop])
        _o = jnp.argsort(dst, stable=True)
        src = src[_o]
        dst = dst[_o]
        edge_attr_64 = 1.36993e-05 + 0.999972 * jax.random.normal(jax.random.fold_in(_gk, 12), (53125, 64), jnp.float32)
        edge_attr_9 = 0.000739051 + 0.999958 * jax.random.normal(jax.random.fold_in(_gk, 13), (53125, 9), jnp.float32)
        return (x, src, dst, edge_attr_64, edge_attr_9)
    x, src, dst, edge_attr_64, edge_attr_9 = _rec_inputs()

    def _L0_gnn_setup():
        import jax, jax.numpy as jnp
        import numpy as np
        N_NODES = 3125
        N_EDGES = 50000
        D = 64
        key = jax.random.key(seed)
        ks = jax.random.split(key, 6)
        feat = jax.random.normal(ks[0], (N_NODES, D), dtype=jnp.float32)
        src = jax.random.randint(ks[1], (N_EDGES,), 0, N_NODES, dtype=jnp.int32)
        dst = jax.random.randint(ks[2], (N_EDGES,), 0, N_NODES, dtype=jnp.int32)
        W1 = jax.random.normal(ks[3], (D, D), dtype=jnp.float32) * (1.0 / np.sqrt(D))
        b1 = jnp.zeros((D,), dtype=jnp.float32)
        W2 = jax.random.normal(ks[4], (D, D), dtype=jnp.float32) * (1.0 / np.sqrt(D))
        b2 = jnp.zeros((D,), dtype=jnp.float32)
        return {'feat': feat, 'src': src, 'dst': dst, 'W1': W1, 'b1': b1, 'W2': W2, 'b2': b2}
    _L0_gnn_all = _L0_gnn_setup()
    _L0_gnn_in = {k: v for k, v in _L0_gnn_all.items() if k in ('W1', 'b1', 'W2', 'b2')}
    del _L0_gnn_all

    def _L1_gnn_setup():
        import jax, jax.numpy as jnp
        import numpy as np
        N, E = (10000, 10000)
        D, S, HE = (64, 9, 64)
        H, DQK, DV = (8, 16, 16)
        OK, OV = (H * DQK, H * DV)
        EPS_BN = 1e-05

        def tensor_product(x_e, sh, w, C):
            acc = sh[:, 0:1] * (x_e @ C[:, 0, :])
            for s in range(1, S):
                acc = acc + sh[:, s:s + 1] * (x_e @ C[:, s, :])
            return acc * w

        def mlp2(x, w1, b1, w2, b2):
            return jax.nn.relu(x @ w1 + b1) @ w2 + b2
        key = jax.random.key(seed)
        ks = jax.random.split(key, 20)
        g = lambda k, shape, fan: jax.random.normal(k, shape, jnp.float32) / np.float32(np.sqrt(fan))
        return {'tfn_features': jax.random.normal(ks[0], (N, D), jnp.float32), 'edge_features': jax.random.normal(ks[1], (E, HE), jnp.float32), 'edge_sh': jax.random.normal(ks[2], (E, S), jnp.float32), 'Wq': g(ks[3], (D, OK), D), 'Cqk': g(ks[4], (D, S, OK), D * S), 'Cv': g(ks[5], (D, S, OV), D * S), 'k_w1': g(ks[6], (HE, HE), HE), 'k_b1': jnp.zeros((HE,), jnp.float32), 'k_w2': g(ks[7], (HE, OK), HE), 'k_b2': jnp.zeros((OK,), jnp.float32), 'v_w1': g(ks[8], (HE, HE), HE), 'v_b1': jnp.zeros((HE,), jnp.float32), 'v_w2': g(ks[9], (HE, OV), HE), 'v_b2': jnp.zeros((OV,), jnp.float32), 'W_out': g(ks[10], (OV, D), OV), 'W_self': g(ks[11], (D, D), D), 'gamma': jnp.ones((D,), jnp.float32), 'beta': jnp.zeros((D,), jnp.float32), 'edge_index': jax.random.randint(ks[12], (2, E), 0, N, dtype=jnp.int32)}
    _L1_gnn_all = _L1_gnn_setup()
    _L1_gnn_in = {k: v for k, v in _L1_gnn_all.items() if k in ('Wq', 'Cqk', 'Cv', 'k_w1', 'k_b1', 'k_w2', 'k_b2', 'v_w1', 'v_b1', 'v_w2', 'v_b2', 'W_out', 'W_self', 'gamma', 'beta')}
    del _L1_gnn_all
    return {'x': x, 'src': src, 'dst': dst, 'edge_attr_64': edge_attr_64, 'edge_attr_9': edge_attr_9, 'L0_gnn_W1': _L0_gnn_in['W1'], 'L0_gnn_b1': _L0_gnn_in['b1'], 'L0_gnn_W2': _L0_gnn_in['W2'], 'L0_gnn_b2': _L0_gnn_in['b2'], 'L1_gnn_Wq': _L1_gnn_in['Wq'], 'L1_gnn_Cqk': _L1_gnn_in['Cqk'], 'L1_gnn_Cv': _L1_gnn_in['Cv'], 'L1_gnn_k_w1': _L1_gnn_in['k_w1'], 'L1_gnn_k_b1': _L1_gnn_in['k_b1'], 'L1_gnn_k_w2': _L1_gnn_in['k_w2'], 'L1_gnn_k_b2': _L1_gnn_in['k_b2'], 'L1_gnn_v_w1': _L1_gnn_in['v_w1'], 'L1_gnn_v_b1': _L1_gnn_in['v_b1'], 'L1_gnn_v_w2': _L1_gnn_in['v_w2'], 'L1_gnn_v_b2': _L1_gnn_in['v_b2'], 'L1_gnn_W_out': _L1_gnn_in['W_out'], 'L1_gnn_W_self': _L1_gnn_in['W_self'], 'L1_gnn_gamma': _L1_gnn_in['gamma'], 'L1_gnn_beta': _L1_gnn_in['beta']}

def reference(x, src, dst, edge_attr_64, edge_attr_9, L0_gnn_W1, L0_gnn_b1, L0_gnn_W2, L0_gnn_b2, L1_gnn_Wq, L1_gnn_Cqk, L1_gnn_Cv, L1_gnn_k_w1, L1_gnn_k_b1, L1_gnn_k_w2, L1_gnn_k_b2, L1_gnn_v_w1, L1_gnn_v_b1, L1_gnn_v_w2, L1_gnn_v_b2, L1_gnn_W_out, L1_gnn_W_self, L1_gnn_gamma, L1_gnn_beta):
    import jax
    import jax.numpy as jnp

    def _L0_gnn_ref(feat, src, dst, W1, b1, W2, b2):
        import jax, jax.numpy as jnp
        import numpy as np
        N_NODES = 3125
        N_EDGES = 50000
        D = 64
        n = feat.shape[0]
        msgs = feat[src]
        agg = jax.ops.segment_sum(msgs, dst, num_segments=n)
        h = agg + feat
        h = jax.nn.relu(h @ W1 + b1)
        h = h @ W2 + b2
        return h

    def _L1_gnn_ref(tfn_features, edge_features, edge_sh, Wq, Cqk, Cv, k_w1, k_b1, k_w2, k_b2, v_w1, v_b1, v_w2, v_b2, W_out, W_self, gamma, beta, edge_index):
        import jax, jax.numpy as jnp
        import numpy as np
        N, E = (10000, 10000)
        D, S, HE = (64, 9, 64)
        H, DQK, DV = (8, 16, 16)
        OK, OV = (H * DQK, H * DV)
        EPS_BN = 1e-05

        def tensor_product(x_e, sh, w, C):
            acc = sh[:, 0:1] * (x_e @ C[:, 0, :])
            for s in range(1, S):
                acc = acc + sh[:, s:s + 1] * (x_e @ C[:, s, :])
            return acc * w

        def mlp2(x, w1, b1, w2, b2):
            return jax.nn.relu(x @ w1 + b1) @ w2 + b2
        edge_dst, edge_src = (edge_index[0], edge_index[1])
        n = tfn_features.shape[0]
        q = (tfn_features @ Wq).reshape(n, H, DQK)
        x_dst = tfn_features[edge_dst]
        wk = mlp2(edge_features, k_w1, k_b1, k_w2, k_b2)
        wv = mlp2(edge_features, v_w1, v_b1, v_w2, v_b2)
        k = tensor_product(x_dst, edge_sh, wk, Cqk).reshape(-1, H, DQK)
        v = tensor_product(x_dst, edge_sh, wv, Cv).reshape(-1, H, DV)
        attn = jnp.einsum('ehd,ehd->eh', q[edge_src], k)
        amax = jax.ops.segment_max(attn, edge_src, num_segments=n)
        ex = jnp.exp(attn - amax[edge_src])
        denom = jax.ops.segment_sum(ex, edge_src, num_segments=n)
        alpha = ex / (denom[edge_src] + 1e-16)
        upd = jax.ops.segment_sum(v * alpha[..., None], edge_src, num_segments=n)
        upd = upd.reshape(n, OV) @ W_out
        out = tfn_features @ W_self + upd
        mu = out.mean(axis=0)
        var = out.var(axis=0)
        return (out - mu) * jax.lax.rsqrt(var + EPS_BN) * gamma + beta
    edge_index = jnp.stack([src, dst])
    x = _layernorm(x + _L0_gnn_ref(x, src, dst, L0_gnn_W1, L0_gnn_b1, L0_gnn_W2, L0_gnn_b2), axis=-1)
    x = _layernorm(x + _L1_gnn_ref(x, edge_attr_64, edge_attr_9, L1_gnn_Wq, L1_gnn_Cqk, L1_gnn_Cv, L1_gnn_k_w1, L1_gnn_k_b1, L1_gnn_k_w2, L1_gnn_k_b2, L1_gnn_v_w1, L1_gnn_v_b1, L1_gnn_v_w2, L1_gnn_v_b2, L1_gnn_W_out, L1_gnn_W_self, L1_gnn_gamma, L1_gnn_beta, edge_index), axis=-1)
    return x

_drawn_inputs = setup_inputs


def setup_inputs(seed=0):
    import zlib

    import numpy as np

    out = dict(_drawn_inputs(seed))
    spreads = {'L0_gnn_b1': (0.0, 0.277),
     'L0_gnn_b2': (0.0, 0.1),
     'L1_gnn_k_b1': (0.0, 0.1),
     'L1_gnn_k_b2': (0.0, 0.1),
     'L1_gnn_v_b1': (0.0, 0.1),
     'L1_gnn_v_b2': (0.0, 0.1),
     'L1_gnn_gamma': (1.0, 0.2),
     'L1_gnn_beta': (0.0, 0.1)}
    factors = {}
    for name, (base, spread) in spreads.items():
        noise = np.random.default_rng([zlib.crc32(name.encode()), seed]).standard_normal(out[name].shape)
        drawn = base * np.exp(spread * noise) if base else spread * noise
        out[name] = jnp.asarray(drawn.astype(out[name].dtype))
    for name, factor in factors.items():
        out[name] = (out[name] * factor).astype(out[name].dtype)
    return out
```

```python
from contextlib import ExitStack

import concourse.bass as bass
from concourse import mybir


def gnn_kernel(nc, x, src, dst, edge_feat, edge_sh, gin_w1, gin_b1, gin_w2, gin_b2, wq, cqk, cv,
               k_w1, k_b1, k_w2, k_b2, v_w1, v_b1, v_w2, v_b2, w_out, w_self, gamma, beta, out):
    fp32, bf16, int32 = mybir.dt.float32, mybir.dt.bfloat16, mybir.dt.int32
    ALU = mybir.AluOpType
    ACT = mybir.ActivationFunctionType
    AX = mybir.AxisListType.X
    ds = bass.ds

    P = 128
    N, D = x.shape
    E, S = edge_sh.shape
    OK = wq.shape[1]
    O2 = 2 * OK
    H = 8
    DH = OK // H
    EPS = 1e-5
    TG = 4
    GE = TG * P
    GROUPS = -(-E // GE)
    TILES = GROUPS * TG
    FULL_T = E // P
    REST = E - FULL_T * P
    BLOCKS = -(-N // P)
    FULL_B = N // P
    REST_N = N - FULL_B * P
    STEPS = GROUPS + BLOCKS - 1
    RT = TILES // TG
    CH = P // H
    CT = TILES // CH
    L = CT * P
    SP2 = (S + 1) // 2
    BIG = 1e38
    AW = OK + H
    assert D == 64 and TILES % CH == 0 and STEPS % 2 == 0 and GROUPS % 2 == 0 and FULL_T == TILES - 1
    NB4 = -(-BLOCKS // 4)

    x1_dram = nc.dram_tensor("x1_rows", [BLOCKS * P, D], fp32, kind="Internal").ap()
    q_dram = nc.dram_tensor("q_rows", [BLOCKS * P, OK], fp32, kind="Internal").ap()
    v_dram = nc.dram_tensor("v_rows", [GROUPS, TG, P, OK], fp32, kind="Internal").ap()

    ctx = ExitStack()
    with ctx:
        def sb(name, shape, dt=fp32):
            return ctx.enter_context(nc.sbuf_tensor(name, shape, dt))

        def sem(name):
            return ctx.enter_context(nc.semaphore(name))

        ident = sb("ident", [P, P])
        iota = sb("iota", [P, P])
        block_base = sb("block_base", [P, BLOCKS])
        step_tab = sb("step_tab", [1, 2, STEPS], int32)
        src_idx = sb("src_idx", [P, TILES + 2 * TG], int32)
        dst_idx = sb("dst_idx", [P, TILES + 2 * TG], int32)
        dst_f = sb("dst_f", [P, TILES])
        sh = sb("sh", [P, S, TILES])
        acc = sb("acc", [P, BLOCKS, AW])
        x_sb = sb("x_sb", [P, BLOCKS, D])
        c_sb = sb("c_sb", [P, SP2, O2])
        w1kv = sb("w1kv", [P, 2, P])
        b1kv = sb("b1kv", [P, 1])
        w2kv = sb("w2kv", [P, O2])
        b2row = sb("b2row", [3, O2])
        b2part = sb("b2part", [3, O2], bf16)
        b2tmp = sb("b2tmp", [3, 3, O2])
        b2hi = sb("b2hi", [3, O2], bf16)
        ones3 = sb("ones3", [3, P], bf16)
        gw1 = sb("gw1", [D, D])
        gb1 = sb("gb1", [D, 1])
        gw2 = sb("gw2", [D + 1, D])
        wq_sb = sb("wq_sb", [D, OK])
        wout_sb = sb("wout_sb", [OK, D])
        wself_sb = sb("wself_sb", [D, D])
        gamma_sb = sb("gamma_sb", [P, D])
        beta_sb = sb("beta_sb", [P, D])
        ones_sq = sb("ones_sq", [P, P])
        stat = sb("stat", [P, 4, BLOCKS])
        colst = sb("colst", [P, 4, D])
        idx_x = sb("idx_x", [P, 2, TG], int32)
        idx_q = sb("idx_q", [P, 2, TG], int32)
        x_ring = sb("x_ring", [P, 2, TG, D])
        w_ring = sb("w_ring", [P, 2, O2])
        onehot = sb("onehot", [P, 2, TG, P])
        dst_rel = sb("dst_rel", [P, 2, TG])
        rows = sb("rows", [1, 5, P])
        col = sb("col", [P, 6])
        one = sb("one", [1, 1])
        gfirst = sb("gfirst", [GROUPS - 1, 1], int32)
        gcol = sb("gcol", [GROUPS - 1, 2])
        gle = sb("gle", [GROUPS - 1, STEPS])
        step_f = sb("step_f", [1, 3, STEPS])

        region = sb("region", [P, TILES * D])
        x_all = region[:, :].rearrange("p (g k d) -> p g k d", g=GROUPS, k=TG)
        at = [0]

        def carve(n):
            at[0] += n
            assert at[0] <= TILES * D
            return region[:, at[0] - n:at[0]]

        logit = carve(TILES * H)
        x1T = carve(BLOCKS * P)[0:D, :]
        x1 = carve(BLOCKS * D).rearrange("p (b d) -> p b d", b=BLOCKS)
        rings_at = at[0]
        q_ring = carve(2 * TG * OK).rearrange("p (u k o) -> p u k o", u=2, k=TG)
        ef_ring = carve(2 * TG * D).rearrange("p (u k d) -> p u k d", u=2, k=TG)
        z_ring = carve(2 * S * D).rearrange("p (r s d) -> p r s d", r=2, s=S)
        zT_ring = carve(2 * SP2 * P).rearrange("p (r j e) -> p r j e", r=2, j=SP2)
        kv_ring = carve(2 * TG * O2).rearrange("p (u k o) -> p u k o", u=2, k=TG)
        kq = carve(TG * OK).rearrange("p (k o) -> p k o", k=TG)
        efT = carve(GE // 2)
        hT_ring = carve(2 * GE).rearrange("p (u e) -> p u e", u=2)
        flags_at = at[0]
        seg = carve(L + 2).bitcast(int32)
        bound_f = carve(L)
        bound_b = carve(L)
        at[0] = rings_at
        a_row = carve(L)
        f_row = carve(L)
        assert at[0] <= flags_at
        m_row = bound_f
        at[0] = flags_at
        y = carve(BLOCKS * D).rearrange("p (b d) -> p b d", b=BLOCKS)
        y2 = carve(BLOCKS * D).rearrange("p (b d) -> p b d", b=BLOCKS)
        q_all = carve(BLOCKS * OK).rearrange("p (b o) -> p b o", b=BLOCKS)
        nT = carve(2 * GE).rearrange("p (u e) -> p u e", u=2)
        nT2 = carve(2 * GE).rearrange("p (u e) -> p u e", u=2)
        at[0] = flags_at
        v_ring = carve(2 * TG * OK).rearrange("p (u k o) -> p u k o", u=2, k=TG)
        wx_ring = carve(2 * TG * AW).rearrange("p (u k o) -> p u k o", u=2, k=TG)
        assert at[0] <= flags_at + L + 2
        at[0] = rings_at
        upd = carve(BLOCKS * OK).rearrange("p (b o) -> p b o", b=BLOCKS)
        updT = carve(2 * GE).rearrange("p (u e) -> p u e", u=2)
        o1 = carve(BLOCKS * D).rearrange("p (b d) -> p b d", b=BLOCKS)
        o2 = carve(BLOCKS * D).rearrange("p (b d) -> p b d", b=BLOCKS)
        at[0] = TILES * D - TG * P * S - 2 * TG * P
        sh_stage = carve(TG * P * S)[0:RT, :].rearrange("r (b n) -> r b n", b=TG)
        dst_stage = carve(TG * P)[0:RT, :].bitcast(int32).rearrange("r (b n) -> r b n", b=TG)
        src_stage = carve(TG * P)[0:RT, :].bitcast(int32).rearrange("r (b n) -> r b n", b=TG)
        stage_f = hT_ring[0:RT, :, :]

        bank = [ctx.enter_context(nc.psum_tensor(f"bank{i}", [P, 512], fp32)) for i in range(8)]

        fills = sem("fills")
        ident_ok = sem("ident_ok")
        load_idx = sem("load_idx")
        load_sh = sem("load_sh")
        load_first = sem("load_first")
        load_w = sem("load_w")
        stage_cast = sem("stage_cast")
        turned = sem("turned")
        turned_used = [sem(f"turned_used{i}") for i in range(2)]
        idx_done = sem("idx_done")
        tab_mm = sem("tab_mm")
        tab_ok = sem("tab_ok")
        gle_ok = sem("gle_ok")
        b2_ok = sem("b2_ok")
        idx0 = [sem(f"idx0_{u}") for u in range(2)]
        got0 = [sem(f"got0_{u}") for u in range(2)]
        x_kept = sem("x_kept")
        oh_ok = sem("oh_ok")
        mm0 = [sem(f"mm0_{u}") for u in range(2)]
        add0 = [sem(f"add0_{u}") for u in range(2)]
        dve_c = sem("dve_c")
        h_ok = sem("h_ok")
        n_pe = sem("n_pe")
        n_act = sem("n_act")
        n_dve = sem("n_dve")
        x1_ok = sem("x1_ok")
        sq_ok = sem("sq_ok")
        x1_stored = sem("x1_stored")
        q_ok = sem("q_ok")
        idxx_ok = sem("idxx_ok")
        idx1 = [sem(f"idx1_{u}") for u in range(2)]
        got1 = [sem(f"got1_{u}") for u in range(2)]
        kq_done = [sem(f"kq_done{u}") for u in range(2)]
        ef_got = [sem(f"ef_got{u}") for u in range(2)]
        ef_turned = [sem(f"ef_turned{u}") for u in range(2)]
        efT_ok = sem("efT_ok")
        h1_mm = sem("h1_mm")
        h1_ok = sem("h1_ok")
        z_ok = sem("z_ok")
        z_turned = sem("z_turned")
        zT_ok = sem("zT_ok")
        w_mm = sem("w_mm")
        w_ok = sem("w_ok")
        main_mm = sem("main_mm")
        kv_ok = [sem(f"kv_ok{r}") for r in range(2)]
        kqm_ok = sem("kqm_ok")
        v_stored = [sem(f"v_stored{u}") for u in range(2)]
        seg_fill = sem("seg_fill")
        seg_got = sem("seg_got")
        lg_ok = sem("lg_ok")
        sm_pe = sem("sm_pe")
        sm_used = sem("sm_used")
        row_mm = sem("row_mm")
        col_mm = sem("col_mm")
        row_ok = sem("row_ok")
        sub_ok = sem("sub_ok")
        exp_ok = sem("exp_ok")
        back_mm = sem("back_mm")
        e_ok = sem("e_ok")
        flags_ok = sem("flags_ok")
        v_got = [sem(f"v_got{u}") for u in range(2)]
        wx_v = [sem(f"wx_v{u}") for u in range(2)]
        wx_e = [sem(f"wx_e{u}") for u in range(2)]
        oh1 = [sem(f"oh1_{u}") for u in range(2)]
        mm1 = [sem(f"mm1_{u}") for u in range(2)]
        add1 = [sem(f"add1_{u}") for u in range(2)]
        rel_ok = sem("rel_ok")
        upd_ok = sem("upd_ok")
        f_pe = sem("f_pe")
        f_act = sem("f_act")
        f_dve = sem("f_dve")
        d_ok = sem("d_ok")
        var_mm = sem("var_mm")
        std_ok = sem("std_ok")
        var_ok = sem("var_ok")
        out_ok = sem("out_ok")
        stored = sem("stored")

        N_FILLS = 16
        TURN_B = 2 + S

        def need(eng, signal, value):
            if not isinstance(value, int) or value > 0:
                eng.wait_ge(signal, value)

        block = ctx.enter_context(nc.Block())

        @block.gpsimd
        def _(pool):
            pool.memset(dst_stage[:, :, :], -1).then_inc(fills, 1)
            pool.memset(src_stage[:, :, :], 0).then_inc(fills, 1)
            pool.memset(sh_stage[:, TG - 1, :], 0.0).then_inc(fills, 1)
            pool.memset(x_sb[:, FULL_B, :], 0.0).then_inc(fills, 1)
            pool.memset(w2kv[:, :], 0.0).then_inc(fills, 1)
            pool.memset(w1kv[:, :, :], 0.0).then_inc(fills, 1)
            pool.memset(ident[:, :], 0.0).then_inc(ident_ok, 1)
            pool.wait_ge(ident_ok, 1)
            pool.affine_select(out=ident[:, :], in_=ident[:, :], compare_op=ALU.not_equal, fill=1.0, base=0,
                               pattern=[[-1, P]], channel_multiplier=1).then_inc(ident_ok, 1)
            pool.iota(iota[:, :], pattern=[[1, P]], base=0, channel_multiplier=0,
                      allow_small_or_imprecise_dtypes=True).then_inc(fills, 1)
            pool.iota(block_base[:, :], pattern=[[P, BLOCKS]], base=0, channel_multiplier=0,
                      allow_small_or_imprecise_dtypes=True).then_inc(fills, 1)
            pool.iota(step_f[:, 0, :], pattern=[[1, STEPS]], base=0, channel_multiplier=0,
                      allow_small_or_imprecise_dtypes=True).then_inc(fills, 1)
            pool.iota(gcol[:, 0:1], pattern=[[0, 1]], base=1, channel_multiplier=1,
                      allow_small_or_imprecise_dtypes=True).then_inc(fills, 1)
            pool.memset(ones_sq[:, :], 1.0).then_inc(fills, 1)
            pool.memset(one[:, :], 1.0).then_inc(fills, 1)
            pool.memset(ones3[:, :], 1.0).then_inc(fills, 1)
            pool.memset(src_idx[:, TILES:TILES + 2 * TG], 0).then_inc(fills, 1)
            pool.memset(dst_idx[:, TILES:TILES + 2 * TG], 0).then_inc(fills, 1)
            pool.memset(acc[:, :, :], 0.0).then_inc(fills, 1)

            with pool.Fori(1, GROUPS // 2 + 1) as turn:
                for u in range(2):
                    pool.wait_ge(ident_ok, 2)
                    pool.wait_ge(idx0[u], turn)
                    for k in range(TG):
                        pool.indirect_dma_start(x_ring[:, u, k, :], None, x, bass.IndirectOffsetOnAxis(
                            ap=idx_x[:, u, k:k + 1], axis=0)).then_inc(got0[u], 16)

            pool.wait_ge(x1_stored, 32)
            with pool.Fori(1, GROUPS // 2 + 1) as turn:
                for u in range(2):
                    pool.wait_ge(x1_stored, 32)
                    pool.wait_ge(idx1[u], turn)
                    for k in range(TG):
                        pool.indirect_dma_start(x_ring[:, u, k, :], None, x1_dram, bass.IndirectOffsetOnAxis(
                            ap=idx_x[:, u, k:k + 1], axis=0)).then_inc(got1[u], 16)
                    for k in range(TG):
                        pool.indirect_dma_start(q_ring[:, u, k, :], None, q_dram, bass.IndirectOffsetOnAxis(
                            ap=idx_q[:, u, k:k + 1], axis=0)).then_inc(got1[u], 16)

        @block.sync
        def _(sp):
            sp.wait_ge(fills, 6)
            for stage, vec in ((dst_stage, dst), (src_stage, src)):
                full = vec[0:3 * RT * P].rearrange("(b r n) -> r b n", b=3, r=RT)
                sp.dma_start(stage[:, 0:3, :], full).then_inc(load_idx, 16)
                sp.dma_start(stage[0:RT - 1, 3, :], vec[3 * RT * P:FULL_T * P].rearrange("(r n) -> r n", n=P))\
                  .then_inc(load_idx, 16)
                sp.dma_start(stage[RT - 1:RT, 3, 0:REST], vec[FULL_T * P:E].rearrange("(r n) -> r n", r=1))\
                  .then_inc(load_idx, 16)
            sp.dma_start(gfirst[:, :], dst[GE::GE].unsqueeze(1), allow_slow_non_contiguous=True).then_inc(load_first, 16)
            sp.dma_start(sh_stage[:, 0:3, :], edge_sh[0:3 * RT * P, :].rearrange("(b r n) s -> r b (n s)", b=3, r=RT))\
              .then_inc(load_sh, 16)
            sp.dma_start(sh_stage[0:RT - 1, 3, :],
                         edge_sh[3 * RT * P:FULL_T * P, :].rearrange("(r n) s -> r (n s)", n=P)).then_inc(load_sh, 16)
            sp.dma_start(sh_stage[RT - 1:RT, 3, 0:REST * S],
                         edge_sh[FULL_T * P:E, :].rearrange("(r n) s -> r (n s)", r=1)).then_inc(load_sh, 16)
            loads = [
                (x_sb[:, 0:FULL_B, :], x[0:FULL_B * P, :].rearrange("(b p) d -> p b d", p=P)),
                (x_sb[0:REST_N, FULL_B, :], x[FULL_B * P:N, :]),
                (b2row[:, 0:OK], k_b2.partition_broadcast(3)), (b2row[:, OK:O2], v_b2.partition_broadcast(3)),
                (w1kv[0:D, 0, 0:D], k_w1), (w1kv[0:D, 0, D:P], v_w1), (w1kv[D:P, 1, 0:D], k_w1), (w1kv[D:P, 1, D:P], v_w1),
                (b1kv[0:D, :], k_b1.unsqueeze(1)), (b1kv[D:P, :], v_b1.unsqueeze(1)),
                (w2kv[0:D, 0:OK], k_w2), (w2kv[D:P, OK:O2], v_w2),
                (gw1[:, :], gin_w1), (gb1[:, :], gin_b1.unsqueeze(1)),
                (gw2[0:D, :], gin_w2), (gw2[D:D + 1, :], gin_b2.unsqueeze(0)),
                (wq_sb[:, :], wq), (wout_sb[:, :], w_out), (wself_sb[:, :], w_self),
                (gamma_sb[:, :], gamma.partition_broadcast(P)), (beta_sb[:, :], beta.partition_broadcast(P)),
                (c_sb[0:D, :, 0:OK], cqk[:, 0::2, :]), (c_sb[0:D, :, OK:O2], cv[:, 0::2, :]),
                (c_sb[D:P, 0:SP2 - 1, 0:OK], cqk[:, 1::2, :]), (c_sb[D:P, 0:SP2 - 1, OK:O2], cv[:, 1::2, :]),
            ]
            assert len(loads) == N_LOADS
            for to, what in loads:
                sp.dma_start(to, what).then_inc(load_w, 16)

            sp.wait_ge(x1_ok, 1)
            sp.dma_start(x1_dram.rearrange("(b p) d -> p b d", p=P), x1).then_inc(x1_stored, 16)
            sp.wait_ge(q_ok, NB4)
            sp.dma_start(q_dram.rearrange("(b p) o -> p b o", p=P), q_all).then_inc(x1_stored, 16)

            def load_group(g, u, i, last=False):
                need(sp, ef_turned[u], i)
                if not last:
                    sp.dma_start(ef_ring[:, u, :, :], edge_feat[ds(g * GE, GE), :].rearrange("(k p) d -> p k d", p=P))\
                      .then_inc(ef_got[u], 32)
                else:
                    sp.dma_start(ef_ring[:, u, 0:TG - 1, :],
                                 edge_feat[(TILES - TG) * P:FULL_T * P, :].rearrange("(k p) d -> p k d", p=P))\
                      .then_inc(ef_got[u], 16)
                    sp.dma_start(ef_ring[0:REST, u, TG - 1, :], edge_feat[FULL_T * P:E, :]).then_inc(ef_got[u], 16)

            def store_group(g, u, i):
                for r in range(2):
                    sp.wait_ge(kv_ok[r], 2 * g + 2)
                sp.dma_start(v_dram[ds(g, 1)].rearrange("g k p o -> p (g k) o"), kv_ring[:, u, :, OK:O2])\
                  .then_inc(v_stored[u], 16)

            load_group(0, 0, 0)
            sp.wait_ge(seg_fill, 2)
            sp.dma_start(seg[0:H, 1:L + 2], dst[0:L + 1].partition_broadcast(H)).then_inc(seg_got, 16)
            for c in range(1, CH - 1):
                sp.dma_start(seg[H * c:H * c + H, :], dst[L * c - 1:L * (c + 1) + 1].partition_broadcast(H))\
                  .then_inc(seg_got, 16)
            sp.dma_start(seg[P - H:P, 0:E - L * (CH - 1) + 1], dst[L * (CH - 1) - 1:E].partition_broadcast(H))\
              .then_inc(seg_got, 16)

            def two_groups(i):
                load_group(2 * i + 1, 1, i)
                store_group(2 * i, 0, i)
                load_group(2 * i + 2, 0, i + 1)
                store_group(2 * i + 1, 1, i)

            two_groups(0)
            with sp.Fori(1, GROUPS // 2 - 1) as i:
                two_groups(i)
            i = GROUPS // 2 - 1
            load_group(2 * i + 1, 1, i, last=True)
            store_group(2 * i, 0, i)
            store_group(2 * i + 1, 1, i)

            sp.wait_ge(flags_ok, 1)
            for u in range(2):
                sp.wait_ge(v_stored[u], 16 * (GROUPS // 2))

            def two_steps(i):
                for u in range(2):
                    te = sp.value_load(step_tab[0:1, 0, ds(2 * i + u, 1)], min_val=0, max_val=GROUPS - 1)
                    need(sp, wx_v[u], i)
                    sp.dma_start(v_ring[:, u, :, :], v_dram[ds(te, 1)].rearrange("g k p o -> p (g k) o"))\
                      .then_inc(v_got[u], 16)

            two_steps(0)
            with sp.Fori(1, STEPS // 2) as i:
                two_steps(i)

            sp.wait_ge(out_ok, 1)
            sp.dma_start(out[0:FULL_B * P, :].rearrange("(b p) d -> p b d", p=P), o1[:, 0:FULL_B, :])\
              .then_inc(stored, 16)
            sp.dma_start(out[FULL_B * P:N, :], o1[0:REST_N, FULL_B, :]).then_inc(stored, 16)
            sp.wait_ge(stored, 32)

        @block.tensor
        def _(pe):
            def turn(to, what, n):
                return pe.transpose(to, what, ident[0:n, 0:n])

            pe.wait_ge(ident_ok, 2)
            for j in range(TURN_B):
                if j < 2:
                    pe.wait_ge(stage_cast, j + 1)
                if j == 2:
                    pe.wait_ge(load_sh, 48)
                if j >= 2:
                    pe.wait_ge(turned_used[j % 2], j // 2)
                for b in range(TG):
                    if j < 2:
                        rows_in = stage_f[:, j, b * P:(b + 1) * P]
                    else:
                        rows_in = sh_stage[:, b, :].rearrange("r (n s) -> r s n", s=S)[:, j - 2, :]
                    last = turn(bank[j % 2][:, b * RT:(b + 1) * RT], rows_in, RT)
                last.then_inc(turned, 1)
            pe.wait_ge(gle_ok, 1)
            pe.wait_ge(fills, N_FILLS)
            pe.matmul(bank[2][0:1, 0:STEPS], ones_sq[0:GROUPS - 1, 0:1], gle[:, :], start=True, stop=True)\
              .then_inc(tab_mm, 1)

            pe.wait_ge(tab_ok, 1)
            for u in range(2):
                pe.wait_ge(turned_used[u], (TURN_B + 1 - u) // 2)

            def two_steps(i):
                for u in range(2):
                    te = pe.value_load(step_tab[0:1, 0, ds(2 * i + u, 1)], min_val=0, max_val=GROUPS - 1)
                    pe.wait_ge(x_kept, te + 1)
                    pe.wait_ge(oh_ok, TG * (2 * i + u) + TG)
                    need(pe, add0[u], i)
                    for k in range(TG):
                        last = pe.matmul(bank[u][:, 0:D], onehot[:, u, k, :], x_all[:, ds(te, 1), k, :],
                                         start=k == 0, stop=k == TG - 1)
                    last.then_inc(mm0[u], 1)

            two_steps(0)
            with pe.Fori(1, STEPS // 2) as i:
                two_steps(i)

            pe.wait_ge(h_ok, 1)
            pe.wait_ge(load_w, 16 * N_LOADS)
            for m in range(NB4):
                blocks = range(4 * m, min(4 * m + 4, BLOCKS))
                w = P * len(blocks)
                if m:
                    pe.wait_ge(n_act, 2 * m - 1)
                for b in blocks:
                    last = turn(bank[0][0:D, (b - 4 * m) * P:(b - 4 * m + 1) * P], y[:, b, :], P)
                last.then_inc(n_pe, 1)
                pe.wait_ge(n_act, 2 * m + 1)
                pe.matmul(bank[1][0:D, 0:w], gw1[:, :], nT[0:D, m % 2, 0:w], start=True, stop=True).then_inc(n_pe, 1)
                pe.wait_ge(n_act, 2 * m + 2)
                if m >= 2:
                    pe.wait_ge(n_dve, m - 1)
                for b in blocks:
                    o = b - 4 * m
                    last = pe.matmul(bank[2 + m % 2][:, o * D:(o + 1) * D], nT2[0:D + 1, m % 2, o * P:(o + 1) * P],
                                     gw2[:, :], start=True, stop=True)
                last.then_inc(n_pe, 1)
            pe.wait_ge(x1_ok, 1)
            for m in range(NB4):
                blocks = range(4 * m, min(4 * m + 4, BLOCKS))
                if m:
                    pe.wait_ge(n_act, 2 * NB4 + m)
                for b in blocks:
                    last = turn(bank[0][0:D, (b - 4 * m) * P:(b - 4 * m + 1) * P], x1[:, b, :], P)
                last.then_inc(n_pe, 1)
                pe.wait_ge(n_act, 2 * NB4 + m + 1)
                if m >= 2:
                    pe.wait_ge(q_ok, m - 1)
                for b in blocks:
                    o = b - 4 * m
                    last = pe.matmul(bank[2 + m % 2][:, o * P:(o + 1) * P], x1T[:, b * P:(b + 1) * P], wq_sb[:, :],
                                     start=True, stop=True)
                last.then_inc(n_pe, 1)
            pe.wait_ge(b2_ok, 1)
            pe.wait_ge(q_ok, NB4)

            POS = [0, 2, 1, 3]

            def turn_ef(g, u, i):
                pe.wait_ge(ef_got[u], 32 * (i + 1))
                need(pe, h1_ok, g)
                for k in range(0, TG, 2):
                    last = turn(bank[3][:, k // 2 * P:(k // 2 + 1) * P], ef_ring[:, u, k:k + 2, :], P)
                last.then_inc(ef_turned[u], 1)

            def hidden(g):
                pe.wait_ge(efT_ok, g + 1)
                for odd in range(2):
                    last = pe.matmul(bank[3][:, odd * GE // 2:(odd + 1) * GE // 2], w1kv[:, odd, :], efT[:, :],
                                     start=True, stop=True)
                last.then_inc(h1_mm, 1)

            def turn_z(t, r, waits=True):
                pe.wait_ge(z_ok, t + 1)
                if waits:
                    need(pe, zT_ok, 2 * (t - 1))
                for j in range(SP2 - 1):
                    turn(bank[r][:, j * P:(j + 1) * P], z_ring[:, r, 2 * j:2 * j + 2, :], P)
                turn(bank[2 + 5 * r][0:D, 0:P], z_ring[:, r, S - 1, :], P).then_inc(z_turned, 1)

            def main(t, r, u, k, uses):
                need(pe, kv_ok[r], uses)
                need(pe, w_ok, t)
                pe.matmul(bank[4][:, 0:O2], hT_ring[:, u, POS[k] * P:(POS[k] + 1) * P], w2kv[:, :],
                          start=True, stop=False)
                pe.matmul(bank[4][:, 0:O2], ones3[:, :], b2part[:, :],
                          start=False, stop=True).then_inc(w_mm, 1)
                pe.wait_ge(zT_ok, 2 * (t + 1))
                for j in range(SP2):
                    n = P if j < SP2 - 1 else D
                    last = pe.matmul(bank[5 + r][:, 0:O2], zT_ring[0:n, r, j, :], c_sb[0:n, j, :],
                                     start=j == 0, stop=j == SP2 - 1)
                last.then_inc(main_mm, 1)

            def group(g, i, u, last=False):
                for k in range(TG):
                    t = TG * g + k
                    if k == 0 and not last:
                        turn_ef(g + 1, 1 - u, i + u)
                    if not (last and k == TG - 1):
                        turn_z(t + 1, (k + 1) % 2)
                    if k == 0:
                        pe.wait_ge(h1_ok, g + 1)
                    main(t, k % 2, u, k, 4 * i + 2 * u + k // 2)
                    if k == 1 and not last:
                        hidden(g + 1)

            turn_ef(0, 0, 0)
            hidden(0)
            turn_z(0, 0, waits=False)
            for u in range(2):
                group(u, 0, u)
            with pe.Fori(1, GROUPS // 2 - 1) as i:
                for u in range(2):
                    group(2 * i + u, i, u)
            for u in range(2):
                group(GROUPS - 2 + u, GROUPS // 2 - 1, u, last=u == 1)

            NS = -(-CT // 4)
            for m in range(NS):
                pe.wait_ge(lg_ok, m + 1)
                if m >= 2:
                    pe.wait_ge(sm_used, m - 1)
                js = range(4 * m, min(4 * m + 4, CT))
                for j in js:
                    last = turn(bank[m % 2][:, (j - 4 * m) * P:(j - 4 * m + 1) * P], f_row[:, j * P:(j + 1) * P], P)
                last.then_inc(sm_pe, 1)
            for way in range(2):
                pe.wait_ge(row_ok, 2 * way + 1)
                for n in range(3):
                    last = turn(bank[2][0:1, n * P:(n + 1) * P], col[:, n:n + 1], P)
                last.then_inc(row_mm, 1)
                pe.wait_ge(row_ok, 2 * way + 2)
                pe.matmul(bank[3][:, way:way + 1], rows[0:1, 4, :], one[:, :], start=True, stop=True).then_inc(col_mm, 1)
            for m in range(NS):
                js = range(4 * m, min(4 * m + 4, CT))
                pe.wait_ge(exp_ok, m + 1)
                if m >= 2:
                    pe.wait_ge(e_ok, m - 1)
                for j in js:
                    last = turn(bank[m % 2][:, (j - 4 * m) * P:(j - 4 * m + 1) * P], a_row[:, j * P:(j + 1) * P], P)
                last.then_inc(back_mm, 1)

            pe.wait_ge(e_ok, NS)

            def two_sums(i):
                for u in range(2):
                    pe.wait_ge(oh1[u], TG * (i + 1))
                    pe.wait_ge(wx_v[u], i + 1)
                    pe.wait_ge(wx_e[u], i + 1)
                    need(pe, add1[u], i)
                    for k in range(TG):
                        last = pe.matmul(bank[u][:, 0:AW], onehot[:, u, k, :], wx_ring[:, u, k, :],
                                         start=k == 0, stop=k == TG - 1)
                    last.then_inc(mm1[u], 1)

            two_sums(0)
            with pe.Fori(1, STEPS // 2) as i:
                two_sums(i)

            pe.wait_ge(upd_ok, 1)
            for m in range(NB4):
                blocks = range(4 * m, min(4 * m + 4, BLOCKS))
                if m:
                    pe.wait_ge(f_act, m)
                for b in blocks:
                    last = turn(bank[0][:, (b - 4 * m) * P:(b - 4 * m + 1) * P], upd[:, b, :], P)
                last.then_inc(f_pe, 1)
                pe.wait_ge(f_act, m + 1)
                if m >= 2:
                    pe.wait_ge(f_dve, m - 1)
                for b in blocks:
                    o = b - 4 * m
                    pe.matmul(bank[2 + m % 2][:, o * D:(o + 1) * D], updT[:, m % 2, o * P:(o + 1) * P],
                              wout_sb[:, :], start=True, stop=False)
                    last = pe.matmul(bank[2 + m % 2][:, o * D:(o + 1) * D], x1T[:, b * P:(b + 1) * P],
                                     wself_sb[:, :], start=False, stop=True)
                last.then_inc(f_pe, 1)
            for n, (what, sem_in, v_in) in enumerate(((o1, f_dve, NB4), (o2, d_ok, 1))):
                pe.wait_ge(sem_in, v_in)
                for b in range(BLOCKS):
                    nn = P if b < FULL_B else REST_N
                    last = pe.matmul(bank[4][:, n * D:(n + 1) * D], ones_sq[0:nn, :], what[0:nn, b, :],
                                     start=b == 0, stop=b == BLOCKS - 1)
                last.then_inc(var_mm, 1)

        @block.scalar
        def _(act):
            act.wait_ge(fills, N_FILLS)
            for j in range(2, TURN_B):
                act.wait_ge(turned, j + 1)
                act.activation(sh[:, j - 2, :], bank[j % 2][:, 0:TILES], ACT.Copy).then_inc(turned_used[j % 2], 1)

            def stage_src(g, u, done):
                return act.activation(idx_x[:, u, :], src_idx[:, ds(g * TG, TG)], ACT.Copy).then_inc(done, 1)

            for j in range(2):
                act.wait_ge(turned_used[j], (TURN_B + 1 - j) // 2)
            for u in range(2):
                stage_src(u, u, idx0[u])
            with act.Fori(0, GROUPS // 2) as i:
                for u in range(2):
                    act.wait_ge(got0[u], 16 * TG * (i + 1))
                    act.activation(x_all[:, ds(2 * i + u, 1), :, :], x_ring[:, u:u + 1, :, :], ACT.Copy)\
                       .then_inc(x_kept, 1)
                    act.wait_ge(x_kept, 2 * i + u + 1)
                    stage_src(2 * i + u + 2, u, idx0[u])

            for m in range(NB4):
                w = P * (min(4 * m + 4, BLOCKS) - 4 * m)
                act.wait_ge(n_pe, 3 * m + 1)
                act.activation(nT[0:D, m % 2, 0:w], bank[0][0:D, 0:w], ACT.Copy).then_inc(n_act, 1)
                act.wait_ge(n_pe, 3 * m + 2)
                if m == 0:
                    act.wait_ge(h_ok, 1)
                act.activation(nT2[0:D, m % 2, 0:w], bank[1][0:D, 0:w], ACT.Relu, bias=gb1[:, :]).then_inc(n_act, 1)
            act.wait_ge(sq_ok, 1)
            act.activation(stat[:, 2, :], stat[:, 1, :], ACT.Sqrt).then_inc(sq_ok, 1)
            for m in range(NB4):
                w = P * (min(4 * m + 4, BLOCKS) - 4 * m)
                act.wait_ge(n_pe, 3 * NB4 + 2 * m + 1)
                act.activation(x1T[:, 4 * m * P:4 * m * P + w], bank[0][0:D, 0:w], ACT.Copy).then_inc(n_act, 1)

            def ef(u, i, g):
                act.wait_ge(ef_turned[u], i + 1)
                need(act, h1_mm, g)
                act.activation(efT[:, :], bank[3][:, 0:GE // 2], ACT.Copy).then_inc(efT_ok, 1)

            def relu(u, g, main_need):
                act.wait_ge(h1_mm, g + 1)
                if main_need is not None:
                    need(act, main_mm, main_need)
                act.activation(hT_ring[:, u, :], bank[3][:, :], ACT.Relu, bias=b1kv[:, :]).then_inc(h1_ok, 1)

            def copy_z(t, r, waits=True):
                act.wait_ge(z_turned, t + 1)
                if waits:
                    need(act, main_mm, t - 1)
                act.activation(zT_ring[:, r, 0:SP2 - 1, :], bank[r][:, :], ACT.Copy).then_inc(zT_ok, 1)
                act.activation(zT_ring[0:D, r, SP2 - 1, :], bank[2 + 5 * r][0:D, 0:P], ACT.Copy)\
                   .then_inc(zT_ok, 1)

            def group(g, i, u, last=False):
                for k in range(TG):
                    t = TG * g + k
                    if k == 0 and not last:
                        ef(1 - u, i + u, g + 1)
                    if not (last and k == TG - 1):
                        copy_z(t + 1, (k + 1) % 2)
                    act.wait_ge(w_mm, t + 1)
                    act.activation(w_ring[:, k % 2, :], bank[4][:, 0:O2], ACT.Copy).then_inc(w_ok, 1)
                    if k == 1 and not last:
                        relu(1 - u, g + 1, TG * g)

            ef(0, 0, 0)
            relu(0, 0, None)
            copy_z(0, 0, waits=False)
            for u in range(2):
                group(u, 0, u)
            with act.Fori(1, GROUPS // 2 - 1) as i:
                for u in range(2):
                    group(2 * i + u, i, u)
            for u in range(2):
                group(GROUPS - 2 + u, GROUPS // 2 - 1, u, last=u == 1)

            NS = -(-CT // 4)
            lg = logit.rearrange("p (c j h) -> p j c h", c=CH, j=CT)
            for u in range(2):
                act.wait_ge(kq_done[u], GROUPS // 2)
                act.wait_ge(v_stored[u], 16 * (GROUPS // 2))
            for m in range(NS):
                nj = min(4 * m + 4, CT) - 4 * m
                act.activation(f_row[:, 4 * m * P:(4 * m + nj) * P].rearrange("p (j c h) -> p j c h", j=nj, c=CH),
                               lg[:, 4 * m:4 * m + nj, :, :], ACT.Copy).then_inc(lg_ok, 1)
            for m in range(NS):
                w = P * (min(4 * m + 4, CT) - 4 * m)
                act.wait_ge(sm_pe, m + 1)
                act.activation(a_row[:, 4 * m * P:4 * m * P + w], bank[m % 2][:, 0:w], ACT.Copy).then_inc(sm_used, 1)
            for m in range(NS):
                w = P * (min(4 * m + 4, CT) - 4 * m)
                act.wait_ge(sub_ok, m + 1)
                act.activation(a_row[:, 4 * m * P:4 * m * P + w], f_row[:, 4 * m * P:4 * m * P + w], ACT.Exp)\
                   .then_inc(exp_ok, 1)
            for m in range(NS):
                nj = min(4 * m + 4, CT) - 4 * m
                act.wait_ge(back_mm, m + 1)
                act.activation(lg[:, 4 * m:4 * m + nj, :, :],
                               bank[m % 2][:, 0:nj * P].rearrange("p (j c h) -> p j c h", j=nj, c=CH), ACT.Copy)\
                   .then_inc(e_ok, 1)

            act.wait_ge(e_ok, NS)
            wts = logit.rearrange("p (g k h) -> p g k h", g=GROUPS, k=TG)

            def two_steps(i):
                for u in range(2):
                    te = act.value_load(step_tab[0:1, 0, ds(2 * i + u, 1)], min_val=0, max_val=GROUPS - 1)
                    need(act, mm1[u], i)
                    act.activation(wx_ring[:, u:u + 1, :, OK:AW], wts[:, ds(te, 1), :, :], ACT.Copy)\
                       .then_inc(wx_e[u], 1)

            two_steps(0)
            with act.Fori(1, STEPS // 2) as i:
                two_steps(i)

            for m in range(NB4):
                w = P * (min(4 * m + 4, BLOCKS) - 4 * m)
                act.wait_ge(f_pe, 2 * m + 1)
                act.activation(updT[:, m % 2, 0:w], bank[0][:, 0:w], ACT.Copy).then_inc(f_act, 1)
            act.wait_ge(var_ok, 1)
            act.activation(colst[:, 2, :], colst[:, 1, :], ACT.Sqrt).then_inc(std_ok, 1)
            act.wait_ge(var_ok, 2)
            act.activation(stat[:, 2, :], stat[:, 1, :], ACT.Sqrt).then_inc(std_ok, 1)

        @block.vector
        def _(dve):
            n_chain = [0]

            def link(ins):
                n_chain[0] += 1
                ins.then_inc(dve_c, 1)
                dve.wait_ge(dve_c, n_chain[0])

            dve.wait_ge(load_idx, 96)
            for j, stage in enumerate((dst_stage, src_stage)):
                dve.tensor_copy(stage_f[:, j, :], stage.rearrange("r b n -> r (b n)")).then_inc(stage_cast, 1)
            dve.wait_ge(turned, 1)
            dve.tensor_copy(dst_f[:, :], bank[0][:, 0:TILES]).then_inc(turned_used[0], 1)
            dve.wait_ge(turned_used[0], 1)
            dve.tensor_scalar(dst_idx[:, 0:TILES], dst_f[:, :], 0.0, None, ALU.max).then_inc(idx_done, 1)
            dve.wait_ge(turned, 2)
            dve.tensor_copy(src_idx[:, 0:TILES], bank[1][:, 0:TILES]).then_inc(turned_used[1], 1)
            dve.wait_ge(idx_done, 1)
            dve.wait_ge(load_first, 16)
            dve.wait_ge(fills, N_FILLS)
            link(dve.tensor_single_scalar(gfirst[:, :], gfirst[:, :], 7, ALU.arith_shift_right))
            link(dve.tensor_tensor(gcol[:, 1:2], gcol[:, 0:1], gfirst[:, :], ALU.add))
            dve.tensor_scalar(gle[:, :], iota[0:GROUPS - 1, 0:STEPS], gcol[:, 1:2], None, ALU.is_ge).then_inc(gle_ok, 1)
            dve.wait_ge(tab_mm, 1)
            link(dve.tensor_copy(step_f[:, 1, :], bank[2][0:1, 0:STEPS]))
            link(dve.tensor_tensor(step_f[:, 2, :], step_f[:, 0, :], step_f[:, 1, :], ALU.subtract))
            dve.tensor_copy(step_tab[:, :, :], step_f[:, 1:3, :]).then_inc(tab_ok, 1)
            dve.wait_ge(tab_ok, 1)

            with dve.Fori(0, STEPS // 2) as i:
                for u in range(2):
                    te = dve.value_load(step_tab[0:1, 0, ds(2 * i + u, 1)], min_val=0, max_val=GROUPS - 1)
                    tb = dve.value_load(step_tab[0:1, 1, ds(2 * i + u, 1)], min_val=0, max_val=BLOCKS - 1)
                    dve.tensor_scalar(dst_rel[:, u, :], dst_f[:, ds(te * TG, TG)], block_base[:, ds(tb, 1)], None,
                                      ALU.subtract).then_inc(rel_ok, 1)
                    dve.wait_ge(rel_ok, 2 * i + u + 1)
                    for k in range(TG):
                        dve.tensor_scalar(onehot[:, u, k, :], iota[:, :], dst_rel[:, u, k:k + 1], None, ALU.is_equal)\
                           .then_inc(oh_ok, 1)
                    dve.wait_ge(mm0[u], i + 1)
                    dve.tensor_tensor(acc[:, ds(tb, 1), 0:D], acc[:, ds(tb, 1), 0:D], bank[u][:, 0:D].unsqueeze(1), ALU.add)\
                       .then_inc(add0[u], 1)
                    dve.wait_ge(add0[u], i + 1)

            dve.wait_ge(load_w, 16 * N_LOADS)
            link(dve.tensor_tensor(y, acc[:, :, 0:D], x_sb[:, :, :], ALU.add))
            link(dve.memset(nT2[D:D + 1, :, :], 1.0))
            dve.memset(acc[:, :, :], 0.0).then_inc(h_ok, 1)
            link(dve.tensor_copy(b2hi[:, :], b2row[:, :]))
            link(dve.tensor_copy(b2tmp[:, 0, :], b2hi[:, :]))
            link(dve.tensor_tensor(b2tmp[:, 1, :], b2row[:, :], b2tmp[:, 0, :], ALU.subtract))
            link(dve.tensor_copy(b2hi[:, :], b2tmp[:, 1, :]))
            link(dve.tensor_copy(b2tmp[:, 2, :], b2hi[:, :]))
            link(dve.tensor_tensor(b2row[:, :], b2tmp[:, 1, :], b2tmp[:, 2, :], ALU.subtract))
            link(dve.tensor_scalar(b2row[:, :], b2row[:, :], ident[0:3, 2:3], None, ALU.mult))
            link(dve.scalar_tensor_tensor(b2row[:, :], b2tmp[:, 2, :], ident[0:3, 1:2], b2row[:, :], ALU.mult, ALU.add))
            dve.scalar_tensor_tensor(b2part[:, :], b2tmp[:, 0, :], ident[0:3, 0:1], b2row[:, :], ALU.mult, ALU.add)\
               .then_inc(b2_ok, 1)
            for m in range(NB4):
                nb = min(4 * m + 4, BLOCKS) - 4 * m
                dve.wait_ge(n_pe, 3 * m + 3)
                dve.tensor_tensor(y2[:, 4 * m:4 * m + nb, :], x_sb[:, 4 * m:4 * m + nb, :],
                                  bank[2 + m % 2][:, 0:nb * D].rearrange("p (b d) -> p b d", b=nb), ALU.add)\
                   .then_inc(n_dve, 1)
            dve.wait_ge(n_dve, NB4)

            def layer_norm(v, tmp, res, sqrt_ask, sqrt_asked, sqrt_done, done_at, done):
                link(dve.tensor_reduce(stat[:, 0, :], v, AX, ALU.add))
                link(dve.tensor_single_scalar(stat[:, 0, :], stat[:, 0, :], 1.0 / D, ALU.mult))
                link(dve.tensor_tensor(v, v, stat[:, 0, :].unsqueeze(2).broadcast_to([P, BLOCKS, D]), ALU.subtract))
                link(dve.tensor_tensor(tmp, v, v, ALU.mult))
                link(dve.tensor_reduce(stat[:, 1, :], tmp, AX, ALU.add))
                dve.tensor_scalar(stat[:, 1, :], stat[:, 1, :], 1.0 / D, EPS, ALU.mult, ALU.add).then_inc(sqrt_ask, 1)
                dve.wait_ge(sqrt_done, done_at)
                link(dve.reciprocal(stat[:, 3, :], stat[:, 2, :]))
                dve.tensor_tensor(res, v, stat[:, 3, :].unsqueeze(2).broadcast_to([P, BLOCKS, D]), ALU.mult)\
                   .then_inc(done, 1)

            layer_norm(y2, y, x1, sq_ok, 1, sq_ok, 2, x1_ok)
            for m in range(NB4):
                nb = min(4 * m + 4, BLOCKS) - 4 * m
                dve.wait_ge(n_pe, 3 * NB4 + 2 * m + 2)
                dve.tensor_copy(q_all[:, 4 * m:4 * m + nb, :],
                                bank[2 + m % 2][:, 0:nb * P].rearrange("p (b o) -> p b o", b=nb)).then_inc(q_ok, 1)
            dve.wait_ge(x1_stored, 32)
            link(dve.memset(seg[:, :], -1))
            dve.memset(seg[:, L + 1:L + 2], -2).then_inc(seg_fill, 2)

            def stage(g, u):
                dve.tensor_copy(idx_x[:, u, :], src_idx[:, ds(g * TG, TG)]).then_inc(idxx_ok, 1)
                dve.wait_ge(idxx_ok, g + 1)
                dve.tensor_copy(idx_q[:, u, :], dst_idx[:, ds(g * TG, TG)]).then_inc(idx1[u], 1)

            def make_z(t, r, u, k, waits=True):
                if waits:
                    need(dve, z_turned, t - 1)
                dve.tensor_tensor(z_ring[:, r, :, :], x_ring[:, u, k, :].unsqueeze(1).broadcast_to([P, S, D]),
                                  sh[:, :, ds(t, 1)].broadcast_to([P, S, D]), ALU.mult).then_inc(z_ok, 1)

            lgt = logit.rearrange("p (g k h) -> p g k h", g=GROUPS, k=TG)

            def group(g, i, u, last=False):
                for k in range(TG):
                    t = TG * g + k
                    if k < TG - 1:
                        make_z(t + 1, (k + 1) % 2, u, k + 1)
                    elif not last:
                        dve.wait_ge(got1[1 - u], 32 * TG * (i + u + 1))
                        make_z(t + 1, 0, 1 - u, 0)
                    if k == 0:
                        need(dve, v_stored[u], 16 * i)
                    dve.wait_ge(main_mm, t + 1)
                    dve.wait_ge(w_ok, t + 1)
                    dve.tensor_tensor(kv_ring[:, u, k, :], bank[5 + k % 2][:, 0:O2], w_ring[:, k % 2, :],
                                      ALU.mult).then_inc(kv_ok[k % 2], 1)
                dve.wait_ge(kv_ok[1], 2 * (g + 1))
                dve.wait_ge(kv_ok[0], 2 * (g + 1))
                dve.tensor_tensor(kq, kv_ring[:, u, :, 0:OK], q_ring[:, u, :, :], ALU.mult).then_inc(kqm_ok, 1)
                dve.wait_ge(kqm_ok, g + 1)
                dve.tensor_reduce(lgt[:, ds(g, 1), :, :].rearrange("p g k h -> p (g k) h"),
                                  kq.rearrange("p k (h d) -> p k h d", h=H), AX, ALU.add).then_inc(kq_done[u], 1)
                if not last:
                    dve.wait_ge(kq_done[u], i + 1)
                    stage(g + 2, u)

            for u in range(2):
                stage(u, u)
            dve.wait_ge(got1[0], 32 * TG)
            make_z(0, 0, 0, 0, waits=False)
            for u in range(2):
                group(u, 0, u)
            with dve.Fori(1, GROUPS // 2 - 1) as i:
                for u in range(2):
                    group(2 * i + u, i, u)
            for u in range(2):
                group(GROUPS - 2 + u, GROUPS // 2 - 1, u, last=u == 1)

            dve.wait_ge(seg_got, 16 * CH)
            mid = seg[:, 1:L + 1]
            for to, nb in ((bound_f, seg[:, 0:L]), (bound_b, seg[:, 2:L + 2])):
                link(dve.tensor_tensor(to, mid, nb, ALU.is_equal))
                link(dve.tensor_scalar(to, to, 2 * BIG, BIG, ALU.mult, ALU.subtract))
            link(dve.tensor_tensor(col[:, 5:6], seg[:, 1:2], seg[:, L:L + 1], ALU.is_equal))
            dve.tensor_scalar(col[:, 4:5], col[:, 5:6], 2 * BIG, BIG, ALU.mult, ALU.subtract).then_inc(flags_ok, 1)
            dve.wait_ge(flags_ok, 1)
            NS = -(-CT // 4)
            dve.wait_ge(sm_used, NS)
            ends = ((a_row, f_row, bound_f, 0, L - 1, 1), (f_row, m_row, bound_b, L - 1, 0, -1))
            for way, (data, res, bound, first, end, step) in enumerate(ends):
                link(dve.tensor_tensor_scan(res[:, ::step], bound[:, ::step], data[:, ::step], -BIG, ALU.min, ALU.max)
                     if way == 0 else
                     dve.tensor_tensor_scan(res[:, ::-1], bound[:, ::-1], data[:, ::-1], -BIG, ALU.min, ALU.max))
                link(dve.tensor_copy(col[:, 0:1], res[:, end:end + 1]))
                edge = col[:, 2:3]
                link(dve.tensor_copy(edge, bound_f[:, 0:1] if way == 0 else col[:, 3:4]))
                if way == 0:
                    link(dve.tensor_copy(col[:, 3:4], bound_b[:, L - 1:L]))
                dve.tensor_tensor(col[:, 1:2], edge, col[:, 4:5], ALU.min).then_inc(row_ok, 1)
                dve.wait_ge(row_mm, way + 1)
                for n in range(3):
                    link(dve.tensor_copy(rows[0:1, n, :].rearrange("o (h c) -> o h c", c=CH),
                                         bank[2][0:1, n * P:(n + 1) * P].rearrange("o (c h) -> o h c", h=H)))
                if way == 0:
                    link(dve.tensor_tensor_scan(rows[0:1, 3, :], rows[0:1, 1, :], rows[0:1, 0, :], -BIG, ALU.min, ALU.max))
                else:
                    link(dve.tensor_tensor_scan(rows[0:1, 3, ::-1], rows[0:1, 1, ::-1], rows[0:1, 0, ::-1], -BIG,
                                                ALU.min, ALU.max))
                state = rows[0:1, 3, :].rearrange("o (h c) -> o h c", c=CH)
                cont = rows[0:1, 2, :].rearrange("o (h c) -> o h c", c=CH)
                carry = rows[0:1, 4, :].rearrange("o (c h) -> o h c", h=H)
                link(dve.memset(rows[0:1, 4, :], -BIG))
                if way == 0:
                    dve.tensor_tensor(carry[:, :, 1:CH], state[:, :, 0:CH - 1], cont[:, :, 1:CH], ALU.min).then_inc(row_ok, 1)
                else:
                    dve.tensor_tensor(carry[:, :, 0:CH - 1], state[:, :, 1:CH], cont[:, :, 0:CH - 1], ALU.min)\
                       .then_inc(row_ok, 1)
                dve.wait_ge(col_mm, way + 1)
                link(dve.tensor_copy(col[:, 5:6], bank[3][:, way:way + 1]))
                if way == 0:
                    link(dve.tensor_tensor_scan(res, bound, data, col[:, 5:6], ALU.min, ALU.max))
                else:
                    link(dve.tensor_tensor_scan(res[:, ::-1], bound[:, ::-1], data[:, ::-1], col[:, 5:6], ALU.min, ALU.max))
            for m in range(NS):
                a, b = 4 * m * P, min(4 * m + 4, CT) * P
                dve.tensor_tensor(f_row[:, a:b], a_row[:, a:b], m_row[:, a:b], ALU.subtract).then_inc(sub_ok, 1)

            dve.wait_ge(e_ok, NS)
            wts = logit.rearrange("p (g k h) -> p g k h", g=GROUPS, k=TG)

            def prepare(s, u, i, first=False):
                te = dve.value_load(step_tab[0:1, 0, ds(s, 1)], min_val=0, max_val=GROUPS - 1)
                tb = dve.value_load(step_tab[0:1, 1, ds(s, 1)], min_val=0, max_val=BLOCKS - 1)
                dve.tensor_scalar(dst_rel[:, u, :], dst_f[:, ds(te * TG, TG)], block_base[:, ds(tb, 1)], None,
                                  ALU.subtract).then_inc(rel_ok, 1)
                dve.wait_ge(v_got[u], 16 * (i + 1))
                need(dve, mm1[u], i)
                dve.tensor_tensor(wx_ring[:, u, :, 0:OK].rearrange("p k (h d) -> p k h d", h=H),
                                  v_ring[:, u, :, :].rearrange("p k (h d) -> p k h d", h=H),
                                  wts[:, ds(te, 1), :, :].rearrange("p g k h -> p (g k) h").unsqueeze(3)
                                  .broadcast_to([P, TG, H, DH]), ALU.mult).then_inc(wx_v[u], 1)
                dve.wait_ge(rel_ok, STEPS + s + 1)
                for k in range(TG):
                    dve.tensor_scalar(onehot[:, u, k, :], iota[:, :], dst_rel[:, u, k:k + 1], None, ALU.is_equal)\
                       .then_inc(oh1[u], 1)

            def take(s, u, i):
                tb = dve.value_load(step_tab[0:1, 1, ds(s, 1)], min_val=0, max_val=BLOCKS - 1)
                dve.wait_ge(mm1[u], i + 1)
                if u == 1:
                    dve.wait_ge(add1[0], i + 1)
                else:
                    need(dve, add1[1], i)
                dve.tensor_tensor(acc[:, ds(tb, 1), :], acc[:, ds(tb, 1), :], bank[u][:, 0:AW].unsqueeze(1), ALU.add)\
                   .then_inc(add1[u], 1)

            def two_steps(i):
                prepare(2 * i + 1, 1, i)
                take(2 * i, 0, i)
                prepare(2 * i + 2, 0, i + 1)
                take(2 * i + 1, 1, i)

            prepare(0, 0, 0)
            two_steps(0)
            with dve.Fori(1, STEPS // 2 - 1) as i:
                two_steps(i)
            prepare(STEPS - 1, 1, STEPS // 2 - 1)
            take(STEPS - 2, 0, STEPS // 2 - 1)
            take(STEPS - 1, 1, STEPS // 2 - 1)
            dve.wait_ge(add1[1], STEPS // 2)

            link(dve.tensor_single_scalar(acc[:, :, OK:AW], acc[:, :, OK:AW], 1e-16, ALU.add))
            link(dve.reciprocal(acc[:, :, OK:AW], acc[:, :, OK:AW]))
            dve.tensor_tensor(upd.rearrange("p b (h d) -> p b h d", h=H),
                              acc[:, :, 0:OK].rearrange("p b (h d) -> p b h d", h=H),
                              acc[:, :, OK:AW].unsqueeze(3).broadcast_to([P, BLOCKS, H, DH]), ALU.mult).then_inc(upd_ok, 1)
            for m in range(NB4):
                nb = min(4 * m + 4, BLOCKS) - 4 * m
                dve.wait_ge(f_pe, 2 * m + 2)
                dve.tensor_copy(o1[:, 4 * m:4 * m + nb, :],
                                bank[2 + m % 2][:, 0:nb * D].rearrange("p (b d) -> p b d", b=nb)).then_inc(f_dve, 1)
            dve.wait_ge(var_mm, 1)
            link(dve.tensor_single_scalar(colst[:, 0, :], bank[4][:, 0:D], 1.0 / N, ALU.mult))
            link(dve.tensor_tensor(o1, o1, colst[:, 0, :].unsqueeze(1).broadcast_to([P, BLOCKS, D]), ALU.subtract))
            dve.tensor_tensor(o2, o1, o1, ALU.mult).then_inc(d_ok, 1)
            dve.wait_ge(var_mm, 2)
            dve.tensor_scalar(colst[:, 1, :], bank[4][:, D:2 * D], 1.0 / N, EPS, ALU.mult, ALU.add).then_inc(var_ok, 1)
            dve.wait_ge(std_ok, 1)
            link(dve.reciprocal(colst[:, 3, :], colst[:, 2, :]))
            link(dve.tensor_tensor(colst[:, 3, :], colst[:, 3, :], gamma_sb[:, :], ALU.mult))
            link(dve.tensor_tensor(o1, o1, colst[:, 3, :].unsqueeze(1).broadcast_to([P, BLOCKS, D]), ALU.mult))
            link(dve.tensor_tensor(o1, o1, beta_sb[:, :].unsqueeze(1).broadcast_to([P, BLOCKS, D]), ALU.add))
            link(dve.tensor_tensor(o1, o1, x1, ALU.add))
            layer_norm(o1, o2, o1, var_ok, 2, std_ok, 2, out_ok)


N_LOADS = 25

_INS = ['x', 'src', 'dst', 'edge_attr_64', 'edge_attr_9', 'L0_gnn_W1', 'L0_gnn_b1', 'L0_gnn_W2', 'L0_gnn_b2',
        'L1_gnn_Wq', 'L1_gnn_Cqk', 'L1_gnn_Cv', 'L1_gnn_k_w1', 'L1_gnn_k_b1', 'L1_gnn_k_w2', 'L1_gnn_k_b2',
        'L1_gnn_v_w1', 'L1_gnn_v_b1', 'L1_gnn_v_w2', 'L1_gnn_v_b2', 'L1_gnn_W_out', 'L1_gnn_W_self',
        'L1_gnn_gamma', 'L1_gnn_beta']


def kernel(**inputs):
    import numpy as _np
    import concourse.bacc as _bacc
    from concourse import mybir as _mybir
    from concourse.bass_utils import run_bass_kernel_spmd as _run

    nc = _bacc.Bacc("TRN2", target_bir_lowering=False, num_devices=1)
    arrays, args = {}, []
    for name in _INS:
        a = _np.ascontiguousarray(inputs[name])
        arrays[f"in_{name}_dram"] = a
        args.append(nc.dram_tensor(f"in_{name}_dram", a.shape, _mybir.dt.from_np(a.dtype), kind="ExternalInput").ap())
    args.append(nc.dram_tensor("out_0_dram", inputs['x'].shape, _mybir.dt.float32, kind="ExternalOutput").ap())
    gnn_kernel(nc, *args)
    r = _run(nc, [arrays], core_ids=[0])
    return r.results[0]["out_0_dram"]
```
